# Optimizing a Trainium2 kernel written in Bass

```python
import numpy as np
import jax
import jax.numpy as jnp

def _softmax(x, axis=-1):
    return jax.nn.softmax(x, axis=axis)
def _gelu(x):
    return jax.nn.gelu(x, approximate=True)
def _silu(x):
    return jax.nn.silu(x)
def _sigmoid(x):
    return jax.nn.sigmoid(x)
def _layernorm(x, axis=-1, eps=1e-5):
    m = jnp.mean(x, axis=axis, keepdims=True)
    v = jnp.var(x, axis=axis, keepdims=True)
    return (x - m) / jnp.sqrt(v + eps)
def _scatter_add(tgt, idx, src, axis=0):
    return tgt.at[idx].add(src)
def _segment_sum(src, seg, n):
    return jax.ops.segment_sum(src, seg, n)

kernel_name = 'mk_rec_standalone_d1_rec_08f4f0'

def setup_inputs(seed: int = 0):
    np.random.seed(seed)
    _w = jnp.asarray
    def _rec_inputs():
        import jax
        import jax.numpy as jnp
        _rk = jax.random.key(seed)
        r_targets = -0.0002422 + 0.999987 * jax.random.normal(jax.random.fold_in(_rk, 1), (1024, 200, 128), jnp.float32)
        r_history_states = -2.88516e-05 + 0.999852 * jax.random.normal(jax.random.fold_in(_rk, 2), (1024, 200, 128), jnp.float32)
        return r_targets, r_history_states
    r_targets, r_history_states = _rec_inputs()
    def _L0_rec_setup():
        import jax, jax.numpy as jnp
        import numpy as np
        B, T, IN, H = (1024, 200, 128, 128)

        def _linear_params(key, out_dim, in_dim):
            kw, kb = jax.random.split(key)
            bound = 1.0 / np.sqrt(in_dim)
            w = jax.random.uniform(kw, (out_dim, in_dim), jnp.float32, -bound, bound)
            b = jax.random.uniform(kb, (out_dim,), jnp.float32, -bound, bound)
            return (w, b)
        key = jax.random.key(seed)
        ks = jax.random.split(key, 10)
        targets = jax.random.normal(ks[0], (B, T, IN), jnp.float32)
        history_states = jax.random.normal(ks[1], (B, T, H), jnp.float32)
        W_w, W_b = _linear_params(ks[2], H, IN)
        xu_w, xu_b = _linear_params(ks[3], H, H)
        hu_w, hu_b = _linear_params(ks[4], H, H)
        xr_w, xr_b = _linear_params(ks[5], H, H)
        hr_w, hr_b = _linear_params(ks[6], H, H)
        xg_w, xg_b = _linear_params(ks[7], H, H)
        hg_w, hg_b = _linear_params(ks[8], H, H)
        ln2_w, ln2_b = _linear_params(ks[9], H, IN + H)
        return dict(targets=targets, history_states=history_states, W_w=W_w, W_b=W_b, xu_w=xu_w, xu_b=xu_b, hu_w=hu_w, hu_b=hu_b, xr_w=xr_w, xr_b=xr_b, hr_w=hr_w, hr_b=hr_b, xg_w=xg_w, xg_b=xg_b, hg_w=hg_w, hg_b=hg_b, ln2_w=ln2_w, ln2_b=ln2_b)
    _L0_rec_all = _L0_rec_setup()
    _L0_rec_in = {k: v for k, v in _L0_rec_all.items() if k in ('W_w', 'W_b', 'xu_w', 'xu_b', 'hu_w', 'hu_b', 'xr_w', 'xr_b', 'hr_w', 'hr_b', 'xg_w', 'xg_b', 'hg_w', 'hg_b', 'ln2_w', 'ln2_b', )}
    del _L0_rec_all

    return {
        "r_targets": r_targets,
        "r_history_states": r_history_states,
        "L0_rec_W_w": _L0_rec_in["W_w"],
        "L0_rec_W_b": _L0_rec_in["W_b"],
        "L0_rec_xu_w": _L0_rec_in["xu_w"],
        "L0_rec_xu_b": _L0_rec_in["xu_b"],
        "L0_rec_hu_w": _L0_rec_in["hu_w"],
        "L0_rec_hu_b": _L0_rec_in["hu_b"],
        "L0_rec_xr_w": _L0_rec_in["xr_w"],
        "L0_rec_xr_b": _L0_rec_in["xr_b"],
        "L0_rec_hr_w": _L0_rec_in["hr_w"],
        "L0_rec_hr_b": _L0_rec_in["hr_b"],
        "L0_rec_xg_w": _L0_rec_in["xg_w"],
        "L0_rec_xg_b": _L0_rec_in["xg_b"],
        "L0_rec_hg_w": _L0_rec_in["hg_w"],
        "L0_rec_hg_b": _L0_rec_in["hg_b"],
        "L0_rec_ln2_w": _L0_rec_in["ln2_w"],
        "L0_rec_ln2_b": _L0_rec_in["ln2_b"],
    }

def reference(r_targets, r_history_states, L0_rec_W_w, L0_rec_W_b, L0_rec_xu_w, L0_rec_xu_b, L0_rec_hu_w, L0_rec_hu_b, L0_rec_xr_w, L0_rec_xr_b, L0_rec_hr_w, L0_rec_hr_b, L0_rec_xg_w, L0_rec_xg_b, L0_rec_hg_w, L0_rec_hg_b, L0_rec_ln2_w, L0_rec_ln2_b):
    import jax
    import jax.numpy as jnp
    def _L0_rec_ref(targets, history_states, W_w, W_b, xu_w, xu_b, hu_w, hu_b, xr_w, xr_b, hr_w, hr_b, xg_w, xg_b, hg_w, hg_b, ln2_w, ln2_b):
        import jax, jax.numpy as jnp
        import numpy as np
        B, T, IN, H = (1024, 200, 128, 128)

        def _linear_params(key, out_dim, in_dim):
            kw, kb = jax.random.split(key)
            bound = 1.0 / np.sqrt(in_dim)
            w = jax.random.uniform(kw, (out_dim, in_dim), jnp.float32, -bound, bound)
            b = jax.random.uniform(kb, (out_dim,), jnp.float32, -bound, bound)
            return (w, b)
        aw = jnp.einsum('bti,hi->bth', targets, W_w) + W_b
        att = jax.nn.softmax(jnp.sum(aw * history_states, -1, keepdims=True), axis=1)
        xu = jnp.einsum('bth,oh->bto', history_states, xu_w) + xu_b
        xr = jnp.einsum('bth,oh->bto', history_states, xr_w) + xr_b
        xg = jnp.einsum('bth,oh->bto', history_states, xg_w) + xg_b

        def step(h, xs):
            xu_t, xr_t, xg_t, a_t = xs
            u = jax.nn.sigmoid(xu_t + h @ hu_w.T + hu_b) * a_t
            r = jax.nn.sigmoid(xr_t + h @ hr_w.T + hr_b)
            g = jnp.tanh(xg_t + r * (h @ hg_w.T + hg_b))
            h = (1.0 - u) * h + u * g
            return (h, None)
        h0 = jnp.zeros((targets.shape[0], hu_w.shape[0]), targets.dtype)
        xs = (jnp.swapaxes(xu, 0, 1), jnp.swapaxes(xr, 0, 1), jnp.swapaxes(xg, 0, 1), jnp.swapaxes(att, 0, 1))
        h, _ = jax.lax.scan(step, h0, xs)
        out = jnp.concatenate([h, targets[:, 0]], axis=-1) @ ln2_w.T + ln2_b
        return out

    y = _L0_rec_ref(r_targets, r_history_states, L0_rec_W_w, L0_rec_W_b, L0_rec_xu_w, L0_rec_xu_b, L0_rec_hu_w, L0_rec_hu_b, L0_rec_xr_w, L0_rec_xr_b, L0_rec_hr_w, L0_rec_hr_b, L0_rec_xg_w, L0_rec_xg_b, L0_rec_hg_w, L0_rec_hg_b, L0_rec_ln2_w, L0_rec_ln2_b)
    return y


_drawn_inputs = setup_inputs


def setup_inputs(seed=0):
    import zlib

    import numpy as np

    out = dict(_drawn_inputs(seed))
    spreads = {}
    factors = {'L0_rec_xu_b': 8.0,
     'L0_rec_hu_w': 29.171,
     'L0_rec_hu_b': 8.0,
     'L0_rec_xr_w': 8.0,
     'L0_rec_xr_b': 64.0,
     'L0_rec_hr_w': 64.0,
     'L0_rec_hr_b': 64.0,
     'L0_rec_xg_b': 3.087,
     'L0_rec_hg_w': 8.0,
     'L0_rec_hg_b': 6.383}
    for name, (base, spread) in spreads.items():
        noise = np.random.default_rng([zlib.crc32(name.encode()), seed]).standard_normal(out[name].shape)
        drawn = base * np.exp(spread * noise) if base else spread * noise
        out[name] = jnp.asarray(drawn.astype(out[name].dtype))
    for name, factor in factors.items():
        out[name] = (out[name] * factor).astype(out[name].dtype)
    return out
```

```python
from contextlib import ExitStack

import concourse.bass as bass
from concourse import mybir

ALU = mybir.AluOpType
ACT = mybir.ActivationFunctionType
AX = mybir.AxisListType
F32 = mybir.dt.float32
F32R = mybir.dt.float32r

P = 128


def bass_attention_gru(nc, targets, hist, W_w, W_b, xu_w, xu_b, hu_w, hu_b, xr_w, xr_b,
                       hr_w, hr_b, xg_w, xg_b, hg_w, hg_b, ln2_w, ln2_b, out):
    B, T, H = hist.shape
    BLK = B // P
    HALVES = 2
    HB = BLK // HALVES
    N = HB * P
    TC = 4
    BODY = 2 * TC
    ITERS = T // BODY
    UNITS = HALVES * BODY
    CU = HALVES * TC
    TLO = min(T, P)
    THI = T - TLO
    VC = 160
    DMA = 16
    assert H == P and T % BODY == 0 and HB == 4

    hist_v = hist.rearrange("(k p) t h -> p k t h", p=P)
    targets_v = targets.rearrange("(k p) t h -> p k t h", p=P)
    out_v = out.rearrange("(k p) o -> p k o", p=P)
    att_dram = nc.dram_tensor("att_dram", (T, B), F32, kind="Internal").ap()

    with ExitStack() as ctx:
        def sb(name, shape, dt=F32):
            return ctx.enter_context(nc.sbuf_tensor(name, shape, dt))

        def sem(name):
            return ctx.enter_context(nc.semaphore(name))

        bank = [ctx.enter_context(nc.psum_tensor(f"bank{i}", [P, N], F32)) for i in range(8)]

        ident = sb("ident", [P, P])
        ones_row = sb("ones_row", [1, P])
        hist_buf = [sb(f"hist_buf{i}", [P, BLK, TC, H]) for i in range(2)]
        targ_buf = [sb(f"targ_buf{i}", [P, BLK, TC, H]) for i in range(2)]
        att_bc = [sb(f"att_bc{i}", [P, TC, B]) for i in range(2)]
        w_nat = sb("w_nat", [P, 6, H])
        w_hi = sb("w_hi", [P, 6, H], F32R)
        w_lo = sb("w_lo", [P, 6, H], F32R)
        w_att = sb("w_att", [P, H + 1])
        ln2_nat = sb("ln2_nat", [P, 2 * H])
        ln2_T = sb("ln2_T", [P, 2 * H])
        ln2_row = sb("ln2_row", [1, H])
        bias = sb("bias", [P, 8])
        targ0 = sb("targ0", [P, BLK, H])
        targ0_T = sb("targ0_T", [P, B])
        histT = [sb(f"histT{i}", [P, N]) for i in range(2)]
        prod_junk = sb("prod_junk", [P, 2, HB, H])
        s_dots = sb("s_dots", [P, BLK, BODY])
        scores = sb("scores", [P, BLK, T])
        neg_max = sb("neg_max", [P, BLK])
        exp_sum = sb("exp_sum", [P, BLK])
        exp_inv = sb("exp_inv", [P, BLK])
        attT_lo = sb("attT_lo", [TLO, B])
        attT_hi = sb("attT_hi", [THI, B])
        x_hi = [sb(f"x_hi{i}", [P, N], F32R) for i in range(2)]
        x_lo = [sb(f"x_lo{i}", [P, N], F32R) for i in range(2)]
        h_all = [sb(f"h{i}", [P, N]) for i in range(2)]
        h_hi = [sb(f"h_hi{i}", [P, N], F32R) for i in range(2)]
        h_lo = [sb(f"h_lo{i}", [P, N], F32R) for i in range(2)]
        r_sb = [sb(f"r{i}", [P, N]) for i in range(2)]
        u_sb = [sb(f"u{i}", [P, N]) for i in range(2)]
        ua_sb = [sb(f"ua{i}", [P, N]) for i in range(2)]
        rg_sb = [sb(f"rg{i}", [P, N]) for i in range(2)]
        pre_sb = [sb(f"pre{i}", [P, N]) for i in range(2)]
        g_sb = [sb(f"g{i}", [P, N]) for i in range(2)]
        d_sb = [sb(f"d{i}", [P, N]) for i in range(2)]
        m_sb = [sb(f"m{i}", [P, N]) for i in range(2)]
        out_sb = sb("out_sb", [P, BLK, H])

        setup_ps = bank[7]
        tpA = [bank[0], bank[1]]
        vA = [[bank[2], bank[3]], [bank[4], bank[5]]]
        u_ps = [bank[0], bank[3]]
        r_ps = [bank[1], bank[4]]
        xg_ps = [bank[2], bank[5]]
        hg_ps = bank[6]
        tp_ps = bank[7]

        ident_zero = sem("ident_zero")
        ident_ready = sem("ident_ready")
        weights_in = sem("weights_in")
        watt_in = sem("watt_in")
        targ0_in = sem("targ0_in")
        setup_T = sem("setup_T")
        setup_out = sem("setup_out")
        w_hi_ready = sem("w_hi_ready")
        hist_in = [sem(f"hist_in{i}") for i in range(2)]
        targ_in = [sem(f"targ_in{i}") for i in range(2)]
        a_tp = sem("a_tp")
        a_histT = sem("a_histT")
        a_v = sem("a_v")
        a_dots = sem("a_dots")
        a_sum = sem("a_sum")
        sm_max = sem("sm_max")
        sm_exp = sem("sm_exp")
        sm_inv = sem("sm_inv")
        sm_att = sem("sm_att")
        att_tp = sem("att_tp")
        att_T = sem("att_T")
        att_out = sem("att_out")
        att_in = [sem(f"att_in{i}") for i in range(2)]
        tp_done = sem("tp_done")
        xhi_done = sem("xhi_done")
        xlo_done = sem("xlo_done")
        r_mm = sem("r_mm")
        g_mm = sem("g_mm")
        u_mm = sem("u_mm")
        r_done = sem("r_done")
        u_done = sem("u_done")
        ua_done = sem("ua_done")
        rg_done = sem("rg_done")
        pre_done = sem("pre_done")
        g_done = sem("g_done")
        d_done = sem("d_done")
        m_done = sem("m_done")
        h_done = sem("h_done")
        hhi_done = sem("hhi_done")
        hlo_done = sem("hlo_done")
        fin_mm = sem("fin_mm")
        fin_out = sem("fin_out")
        stored = sem("stored")

        block = ctx.enter_context(nc.Block())

        XU, XR, XG, HU, HR, HG = range(6)

        @block.sync
        def _(sp):
            sp.dma_start(w_att[:, 0:H], W_w).then_inc(watt_in, DMA)
            sp.dma_start(w_att[:, H:H + 1], W_b.rearrange("(p a) -> p a", a=1)).then_inc(watt_in, DMA)
            for j, w in enumerate((xu_w, xr_w, xg_w, hu_w, hr_w, hg_w)):
                sp.dma_start(w_nat[:, j, :], w).then_inc(weights_in, DMA)
            for j, b in enumerate((xu_b, hu_b, xr_b, hr_b, xg_b, hg_b)):
                sp.dma_start(bias[:, j:j + 1], b.rearrange("(p a) -> p a", a=1)).then_inc(weights_in, DMA)
            sp.dma_start(ln2_nat[:, :], ln2_w).then_inc(weights_in, DMA)
            sp.dma_start(ln2_row[:, :], ln2_b.rearrange("(a n) -> a n", a=1)).then_inc(weights_in, DMA)
            sp.dma_start(targ0[:, :, :], targets_v[:, :, 0, :]).then_inc(targ0_in, DMA)

            def load_pair(t0, c):
                sp.dma_start(hist_buf[c][:, :, :, :], hist_v[:, :, t0, :]).then_inc(hist_in[c], DMA)
                sp.dma_start(targ_buf[c][:, :, :, :], targets_v[:, :, t0, :]).then_inc(targ_in[c], DMA)

            for c in range(2):
                load_pair(bass.ds(c * TC, TC), c)
            with sp.Fori(1, ITERS) as i:
                for c in range(2):
                    sp.wait_ge(a_tp, i * UNITS - (UNITS - (c + 1) * CU))
                    sp.wait_ge(a_dots, i * UNITS - (UNITS - (c + 1) * CU))
                    load_pair(bass.ds(i * BODY + c * TC, TC), c)

            def load_hist(t0, c):
                sp.dma_start(hist_buf[c][:, :, :, :], hist_v[:, :, t0, :]).then_inc(hist_in[c], DMA)

            def load_att(t0, c):
                sp.dma_start(att_bc[c][:, :, :], att_dram[t0, :].partition_broadcast(P))\
                    .then_inc(att_in[c], DMA)

            for c in range(2):
                sp.wait_ge(a_tp, T * HALVES - UNITS + (c + 1) * CU)
                load_hist(bass.ds(c * TC, TC), c)
            sp.wait_ge(att_T, 2)
            sp.dma_start(att_dram[0:TLO, :], attT_lo[:, :]).then_inc(att_out, DMA)
            sp.dma_start(att_dram[TLO:T, :], attT_hi[:, :]).then_inc(att_out, DMA)
            sp.wait_ge(att_out, 2 * DMA)
            for c in range(2):
                load_att(bass.ds(c * TC, TC), c)
            with sp.Fori(1, ITERS) as i:
                for c in range(2):
                    sp.wait_ge(tp_done, i * UNITS - (UNITS - (c + 1) * CU))
                    load_hist(bass.ds(i * BODY + c * TC, TC), c)
                    sp.wait_ge(ua_done, i * UNITS - (UNITS - (c + 1) * CU))
                    load_att(bass.ds(i * BODY + c * TC, TC), c)

            sp.wait_ge(fin_out, 2)
            sp.dma_start(out_v, out_sb[:, :, :]).then_inc(stored, DMA)
            sp.wait_ge(stored, DMA)

        @block.gpsimd
        def _(pool):
            nc.gpsimd.memset(ident[:, :], 0.0).then_inc(ident_zero, 1)
            pool.wait_ge(ident_zero, 1)
            nc.gpsimd.affine_select(out=ident[:, :], in_=ident[:, :], compare_op=ALU.not_equal, fill=1.0,
                                    base=0, pattern=[[-1, P]], channel_multiplier=1).then_inc(ident_ready, 1)

            def unit(i, j, last):
                n, g, c, tt = i * UNITS + j, j % 2, j // CU, j % CU // 2
                if j % CU == 0:
                    pool.wait_ge(att_in[c], (i + 1) * DMA)
                pool.wait_ge(u_done, n + 1)
                nc.gpsimd.tensor_tensor(ua_sb[g][:, :], u_sb[g][:, :], att_bc[c][:, tt, g * N:(g + 1) * N],
                                        ALU.mult).then_inc(ua_done, 1)
                if not (last and j == UNITS - 1):
                    pool.wait_ge(hhi_done, n + 2)
                    nc.gpsimd.tensor_tensor(h_lo[1 - g][:, :], h_all[1 - g][:, :],
                                            h_hi[1 - g][:, :].bitcast(F32), ALU.subtract).then_inc(hlo_done, 1)

            with pool.Fori(0, ITERS - 1) as i:
                for j in range(UNITS):
                    unit(i, j, False)
            for j in range(UNITS):
                unit(ITERS - 1, j, True)

        @block.tensor
        def _(pe):
            pe.wait_ge(ident_ready, 1)
            pe.wait_ge(weights_in, 14 * DMA)
            for q in range(2):
                if q:
                    pe.wait_ge(setup_out, q)
                for j in range(3):
                    last = nc.tensor.transpose(setup_ps[:, j * H:(j + 1) * H], w_nat[:, 3 * q + j, :], ident[:, :])
                last.then_inc(setup_T, 1)
            pe.wait_ge(setup_out, 2)
            for j in range(2):
                last = nc.tensor.transpose(setup_ps[:, j * H:(j + 1) * H], ln2_nat[:, j * H:(j + 1) * H], ident[:, :])
            last.then_inc(setup_T, 1)
            pe.wait_ge(targ0_in, DMA)
            for q in range(HALVES):
                pe.wait_ge(setup_out, 3 + q)
                for k in range(HB):
                    last = nc.tensor.transpose(setup_ps[:, k * P:(k + 1) * P], targ0[:, q * HB + k, :], ident[:, :])
                last.then_inc(setup_T, 1)

            pe.wait_ge(watt_in, 2 * DMA)

            def transpose_history(j, dst, done):
                g, c, tt = j % 2, j // CU, j % CU // 2
                for k in range(HB):
                    last = nc.tensor.transpose(dst[:, k * P:(k + 1) * P], hist_buf[c][:, g * HB + k, tt, :],
                                               ident[:, :])
                last.then_inc(done, 1)

            with pe.Fori(0, ITERS) as i:
                n0 = i * UNITS
                pe.wait_ge(hist_in[0], (i + 1) * DMA)
                pe.wait_ge(a_sum, i + 1)
                transpose_history(0, tpA[0], a_tp)
                for j in range(UNITS):
                    if j + 1 < UNITS:
                        if j + 1 == CU:
                            pe.wait_ge(hist_in[1], (i + 1) * DMA)
                        if j >= 1:
                            pe.wait_ge(a_histT, n0 + j)
                        transpose_history(j + 1, tpA[(j + 1) % 2], a_tp)
                    pe.wait_ge(a_histT, n0 + (j + 1))
                    if j >= 2:
                        pe.wait_ge(a_dots, n0 + (j - 1))
                    for k in range(HB):
                        last = nc.tensor.matmul(vA[j % 2][k // 2][:, k % 2 * VC:k % 2 * VC + H + 1],
                                                histT[j % 2][:, k * P:(k + 1) * P], w_att[:, :],
                                                start=True, stop=True)
                    last.then_inc(a_v, 1)

            pe.wait_ge(sm_att, 1)
            for k in range(BLK):
                last = nc.tensor.transpose(bank[k // HB][:, k % HB * P:(k % HB + 1) * P], scores[:, k, 0:TLO],
                                           ident[:, :])
            last.then_inc(att_tp, 1)
            for k in range(BLK):
                last = nc.tensor.transpose(bank[2 + k // HB][0:THI, k % HB * P:(k % HB + 1) * P],
                                           scores[:, k, TLO:T], ident[:, :])
            last.then_inc(att_tp, 1)

            def from_history(g):
                for dst, w in ((u_ps[g], XU), (r_ps[g], XR), (xg_ps[g], XG)):
                    nc.tensor.matmul(dst[:, :], w_hi[:, w, :], x_hi[g][:, :], start=True, stop=False)
                    nc.tensor.matmul(dst[:, :], w_lo[:, w, :], x_hi[g][:, :], start=False, stop=False)
                    nc.tensor.matmul(dst[:, :], w_hi[:, w, :], x_lo[g][:, :], start=False, stop=w == XG)

            def unit(i, j, last):
                n, g = i * UNITS + j, j % 2
                pe.wait_ge(hhi_done, n + 1)
                pe.wait_ge(rg_done, n + 1)
                gates = ((r_ps[g], HR), (hg_ps, HG), (u_ps[g], HU))
                for dst, w in gates:
                    nc.tensor.matmul(dst[:, :], w_hi[:, w, :], h_hi[g][:, :], start=w == HG, stop=False)
                    nc.tensor.matmul(dst[:, :], w_lo[:, w, :], h_hi[g][:, :], start=False, stop=False)
                pe.wait_ge(hlo_done, n + 1)
                for (dst, w), ready in zip(gates, (r_mm, g_mm, u_mm)):
                    nc.tensor.matmul(dst[:, :], w_hi[:, w, :], h_lo[g][:, :], start=False, stop=True)\
                        .then_inc(ready, 1)
                if last and j + 1 == UNITS:
                    return
                pe.wait_ge(xlo_done, n + 2)
                if not (last and j + 2 >= UNITS):
                    ahead = (j + 2) % UNITS
                    if ahead % CU == 0:
                        pe.wait_ge(hist_in[ahead // CU], (i + (ITERS + 1 + (j + 2) // UNITS)) * DMA)
                    transpose_history(ahead, tp_ps, tp_done)
                from_history(1 - g)

            pe.wait_ge(att_T, 2)
            pe.wait_ge(setup_out, 5)
            pe.wait_ge(hist_in[0], (ITERS + 1) * DMA)
            transpose_history(0, tp_ps, tp_done)
            pe.wait_ge(xlo_done, 1)
            transpose_history(1, tp_ps, tp_done)
            from_history(0)
            with pe.Fori(0, ITERS - 1) as i:
                for j in range(UNITS):
                    unit(i, j, False)
            for j in range(UNITS):
                unit(ITERS - 1, j, True)

            for g in range(HALVES):
                pe.wait_ge(h_done, T * HALVES + 1 + g)
                pe.wait_ge(pre_done, T * HALVES)
                pe.wait_ge(u_done, T * HALVES)
                for k in range(HB):
                    o = r_ps[g][:, k * P:(k + 1) * P]
                    nc.tensor.matmul(o, h_all[g][:, k * P:(k + 1) * P], ln2_T[:, 0:H], start=True, stop=False)
                    nc.tensor.matmul(o, targ0_T[:, (g * HB + k) * P:(g * HB + k + 1) * P], ln2_T[:, H:2 * H],
                                     start=False, stop=False)
                    last = nc.tensor.matmul(o, ones_row[:, :], ln2_row[:, :], start=False, stop=True)
                last.then_inc(fin_mm, 1)

        @block.scalar
        def _(act):
            for q in range(2):
                act.wait_ge(setup_T, q + 1)
                nc.scalar.activation(w_hi[:, 3 * q:3 * q + 3, :], setup_ps[:, 0:3 * H], ACT.Copy)\
                    .then_inc(w_hi_ready, 1)
            act.wait_ge(setup_T, 3)
            nc.scalar.activation(ln2_T[:, :], setup_ps[:, 0:2 * H], ACT.Copy).then_inc(setup_out, 1)
            for q in range(HALVES):
                act.wait_ge(setup_T, 4 + q)
                nc.scalar.activation(targ0_T[:, q * N:(q + 1) * N], setup_ps[:, :], ACT.Copy)\
                    .then_inc(setup_out, 1)

            def evacuate(n0, j):
                act.wait_ge(a_tp, n0 + (j + 1))
                if j >= 2:
                    act.wait_ge(a_v, n0 + (j - 1))
                nc.scalar.activation(histT[j % 2][:, :], tpA[j % 2][:, :], ACT.Copy).then_inc(a_histT, 1)

            with act.Fori(0, ITERS) as i:
                n0 = i * UNITS
                for j in range(UNITS):
                    evacuate(n0, j)

            act.wait_ge(sm_max, 2)
            for k in range(BLK):
                last = nc.scalar.activation(scores[:, k, :], scores[:, k, :], ACT.Exp,
                                            bias=neg_max[:, k:k + 1], accum_out=exp_sum[:, k:k + 1])
            last.then_inc(sm_exp, 1)
            act.wait_ge(att_tp, 1)
            for q in range(HALVES):
                last = nc.scalar.activation(attT_lo[:, q * N:(q + 1) * N], bank[q][:, :], ACT.Copy)
            last.then_inc(att_T, 1)

            def split_history(n, g):
                act.wait_ge(tp_done, n + 1)
                nc.scalar.activation(x_hi[g][:, :], tp_ps[:, :], ACT.Copy).then_inc(xhi_done, 1)

            def unit(i, j, last):
                n, g = i * UNITS + j, j % 2
                act.wait_ge(r_mm, n + 1)
                nc.scalar.activation(r_sb[g][:, :], r_ps[g][:, :], ACT.Sigmoid, bias=bias[:, 7:8]).then_inc(r_done, 1)
                act.wait_ge(u_mm, n + 1)
                nc.scalar.activation(u_sb[g][:, :], u_ps[g][:, :], ACT.Sigmoid, bias=bias[:, 6:7]).then_inc(u_done, 1)
                if not (last and j == UNITS - 1):
                    act.wait_ge(h_done, n + 2)
                    nc.scalar.activation(h_hi[1 - g][:, :], h_all[1 - g][:, :], ACT.Copy).then_inc(hhi_done, 1)
                if not (last and j + 2 >= UNITS):
                    split_history(n + 2, g)
                act.wait_ge(pre_done, n + 1)
                nc.scalar.activation(g_sb[g][:, :], pre_sb[g][:, :], ACT.Tanh, bias=bias[:, 4:5]).then_inc(g_done, 1)

            split_history(0, 0)
            act.wait_ge(xlo_done, 1)
            split_history(1, 1)
            with act.Fori(0, ITERS - 1) as i:
                for j in range(UNITS):
                    unit(i, j, False)
            for j in range(UNITS):
                unit(ITERS - 1, j, True)

            act.wait_ge(fin_mm, 1)
            nc.scalar.activation(out_sb[:, 0:HB, :], r_ps[0][:, :], ACT.Copy).then_inc(fin_out, 1)

        @block.vector
        def _(dve):
            nc.vector.memset(ones_row[:, :], 1.0).then_inc(a_sum, 1)
            for g in range(HALVES):
                nc.vector.memset(h_all[g][:, :], 0.0).then_inc(h_done, 1)
            nc.vector.memset(h_hi[0][:, :].bitcast(F32), 0.0).then_inc(hhi_done, 1)
            nc.vector.memset(h_lo[0][:, :].bitcast(F32), 0.0).then_inc(hlo_done, 1)
            dve.wait_ge(weights_in, 14 * DMA)
            nc.vector.tensor_tensor(bias[:, 6:8], bias[:, 0:4:2], bias[:, 1:4:2], ALU.add).then_inc(rg_done, 1)
            for q in range(2):
                dve.wait_ge(w_hi_ready, q + 1)
                nc.vector.tensor_tensor(w_lo[:, 3 * q:3 * q + 3, :],
                                        setup_ps[:, 0:3 * H].rearrange("p (j h) -> p j h", j=3),
                                        w_hi[:, 3 * q:3 * q + 3, :].bitcast(F32), ALU.subtract)\
                    .then_inc(setup_out, 1)

            with dve.Fori(0, ITERS) as i:
                n0 = i * UNITS
                for j in range(UNITS):
                    g, c, tt = j % 2, j // CU, j % CU // 2
                    if j % CU == 0:
                        dve.wait_ge(targ_in[c], (i + 1) * DMA)
                    if j == 0:
                        dve.wait_ge(a_sum, i + 1)
                    dve.wait_ge(a_v, n0 + (j + 1))
                    for k in range(HB):
                        v = vA[j % 2][k // 2][:, k % 2 * VC:k % 2 * VC + H + 1]
                        last = nc.vector.tensor_tensor_reduce(
                            out=prod_junk[:, j % 2, k, :], in0=v[:, 0:H],
                            in1=targ_buf[c][:, g * HB + k, tt, :], scale=1.0, scalar=v[:, H:H + 1],
                            op0=ALU.mult, op1=ALU.add, accum_out=s_dots[:, g * HB + k, j // 2:j // 2 + 1])
                    last.then_inc(a_dots, 1)
                dve.wait_ge(a_dots, n0 + UNITS)
                nc.vector.tensor_copy(scores[:, :, bass.ds(i * BODY, BODY)], s_dots[:, :, :]).then_inc(a_sum, 1)

            dve.wait_ge(a_sum, ITERS + 1)
            nc.vector.reduce_max(neg_max[:, :], scores[:, :, :], AX.X).then_inc(sm_max, 1)
            dve.wait_ge(sm_max, 1)
            nc.vector.tensor_scalar(neg_max[:, :], neg_max[:, :], -1.0, None, ALU.mult).then_inc(sm_max, 1)
            dve.wait_ge(sm_exp, 1)
            nc.vector.reciprocal(exp_inv[:, :], exp_sum[:, :]).then_inc(sm_inv, 1)
            dve.wait_ge(sm_inv, 1)
            for k in range(BLK):
                last = nc.vector.tensor_scalar(scores[:, k, :], scores[:, k, :], exp_inv[:, k:k + 1], None, ALU.mult)
            last.then_inc(sm_att, 1)
            dve.wait_ge(att_tp, 2)
            for q in range(HALVES):
                last = nc.vector.tensor_copy(attT_hi[:, q * N:(q + 1) * N], bank[2 + q][0:THI, :])
            last.then_inc(att_T, 1)

            def split_history(n, g):
                dve.wait_ge(xhi_done, n + 1)
                nc.vector.tensor_tensor(x_lo[g][:, :], tp_ps[:, :], x_hi[g][:, :].bitcast(F32), ALU.subtract)\
                    .then_inc(xlo_done, 1)

            def unit(i, j, last):
                n, g = i * UNITS + j, j % 2
                dve.wait_ge(g_mm, n + 1)
                dve.wait_ge(r_done, n + 1)
                nc.vector.scalar_tensor_tensor(out=rg_sb[g][:, :], in0=hg_ps[:, :], scalar=bias[:, 5:6],
                                               in1=r_sb[g][:, :], op0=ALU.add, op1=ALU.mult).then_inc(rg_done, 1)
                dve.wait_ge(rg_done, n + 2)
                nc.vector.tensor_tensor(pre_sb[g][:, :], rg_sb[g][:, :], xg_ps[g][:, :], ALU.add)\
                    .then_inc(pre_done, 1)
                if not (last and j + 2 >= UNITS):
                    split_history(n + 2, g)
                dve.wait_ge(g_done, n + 1)
                nc.vector.tensor_tensor(d_sb[g][:, :], g_sb[g][:, :], h_all[g][:, :], ALU.subtract)\
                    .then_inc(d_done, 1)
                dve.wait_ge(d_done, n + 1)
                dve.wait_ge(ua_done, n + 1)
                nc.vector.tensor_tensor(m_sb[g][:, :], ua_sb[g][:, :], d_sb[g][:, :], ALU.mult).then_inc(m_done, 1)
                dve.wait_ge(m_done, n + 1)
                nc.vector.tensor_tensor(h_all[g][:, :], h_all[g][:, :], m_sb[g][:, :], ALU.add).then_inc(h_done, 1)

            split_history(0, 0)
            split_history(1, 1)
            with dve.Fori(0, ITERS - 1) as i:
                for j in range(UNITS):
                    unit(i, j, False)
            for j in range(UNITS):
                unit(ITERS - 1, j, True)

            dve.wait_ge(fin_mm, 2)
            nc.vector.tensor_copy(out_sb[:, HB:BLK, :], r_ps[1][:, :].rearrange("p (k o) -> p k o", k=HB))\
                .then_inc(fin_out, 1)


_INS = ["r_targets", "r_history_states"] + [
    f"L0_rec_{w}_{k}" for w in ("W", "xu", "hu", "xr", "hr", "xg", "hg", "ln2") for k in "wb"]
_OUT = ((1024, 128), "float32")


def kernel(**inputs):
    import numpy as np
    import concourse.bacc as bacc
    from concourse.bass_utils import run_bass_kernel_spmd

    nc = bacc.Bacc("TRN2", target_bir_lowering=False, num_devices=1)
    arrays, args = {}, []
    for name in _INS:
        a = np.ascontiguousarray(inputs[name])
        arrays[f"in_{name}"] = a
        args.append(nc.dram_tensor(f"in_{name}", a.shape, mybir.dt.from_np(a.dtype), kind="ExternalInput").ap())
    args.append(nc.dram_tensor("out_dram", _OUT[0], mybir.dt.from_np(np.dtype(_OUT[1])), kind="ExternalOutput").ap())
    bass_attention_gru(nc, *args)
    r = run_bass_kernel_spmd(nc, [arrays], core_ids=[0])
    return r.results[0]["out_dram"]
```

```python
from contextlib import ExitStack

import concourse.bass as bass
from concourse import mybir

ALU = mybir.AluOpType
ACT = mybir.ActivationFunctionType
AX = mybir.AxisListType
ENGINE = mybir.EngineType
F32 = mybir.dt.float32
F32R = mybir.dt.float32r

P = 128


def bass_attention_gru(nc, targets, hist, W_w, W_b, xu_w, xu_b, hu_w, hu_b, xr_w, xr_b,
                       hr_w, hr_b, xg_w, xg_b, hg_w, hg_b, ln2_w, ln2_b, out):
    B, T, H = hist.shape
    BLK = B // P
    HALVES = 2
    HB = BLK // HALVES
    N = HB * P
    TC = 4
    BODY = 2 * TC
    ITERS = T // BODY
    UNITS = HALVES * BODY
    CU = HALVES * TC
    TLO = min(T, P)
    THI = T - TLO
    VC = 160
    DMA = 16
    assert H == P and T % BODY == 0 and HB == 4

    hist_v = hist.rearrange("(k p) t h -> p k t h", p=P)
    targets_v = targets.rearrange("(k p) t h -> p k t h", p=P)
    out_v = out.rearrange("(k p) o -> p k o", p=P)
    att_dram = nc.dram_tensor("att_dram", (T, B), F32, kind="Internal").ap()

    with ExitStack() as ctx:
        def sb(name, shape, dt=F32):
            return ctx.enter_context(nc.sbuf_tensor(name, shape, dt))

        def sem(name):
            return ctx.enter_context(nc.semaphore(name))

        bank = [ctx.enter_context(nc.psum_tensor(f"bank{i}", [P, N], F32)) for i in range(8)]

        ident = sb("ident", [P, P])
        ones_row = sb("ones_row", [1, P])
        hist_buf = [sb(f"hist_buf{i}", [P, BLK, TC, H]) for i in range(2)]
        targ_buf = [sb(f"targ_buf{i}", [P, BLK, TC, H]) for i in range(2)]
        att_bc = [sb(f"att_bc{i}", [P, TC, B]) for i in range(2)]
        w_nat = sb("w_nat", [P, 6, H])
        w_hi = sb("w_hi", [P, 6, H], F32R)
        w_lo = sb("w_lo", [P, 6, H], F32R)
        w_att = sb("w_att", [P, H + 1])
        ln2_nat = sb("ln2_nat", [P, 2 * H])
        ln2_T = sb("ln2_T", [P, 2 * H])
        ln2_row = sb("ln2_row", [1, H])
        bias = sb("bias", [P, 8])
        targ0 = sb("targ0", [P, BLK, H])
        targ0_T = sb("targ0_T", [P, B])
        histT = [sb(f"histT{i}", [P, N]) for i in range(2)]
        prod_junk = sb("prod_junk", [P, 2, HB, H])
        s_dots = sb("s_dots", [P, BLK, BODY])
        scores = sb("scores", [P, BLK, T])
        neg_max = sb("neg_max", [P, BLK])
        exp_sum = sb("exp_sum", [P, BLK])
        exp_inv = sb("exp_inv", [P, BLK])
        attT_lo = sb("attT_lo", [TLO, B])
        attT_hi = sb("attT_hi", [THI, B])
        x_hi = [sb(f"x_hi{i}", [P, N], F32R) for i in range(2)]
        x_lo = [sb(f"x_lo{i}", [P, N], F32R) for i in range(2)]
        h_all = [sb(f"h{i}", [P, N]) for i in range(2)]
        h_hi = [sb(f"h_hi{i}", [P, N], F32R) for i in range(2)]
        h_lo = [sb(f"h_lo{i}", [P, N], F32R) for i in range(2)]
        r_sb = [sb(f"r{i}", [P, N]) for i in range(2)]
        u_sb = [sb(f"u{i}", [P, N]) for i in range(2)]
        ua_sb = [sb(f"ua{i}", [P, N]) for i in range(2)]
        rg_sb = [sb(f"rg{i}", [P, N]) for i in range(2)]
        pre_sb = [sb(f"pre{i}", [P, N]) for i in range(2)]
        ug_sb = [sb(f"ug{i}", [P, N]) for i in range(2)]
        out_sb = sb("out_sb", [P, BLK, H])

        setup_ps = bank[7]
        out_setup_ps = bank[6]
        tpA = [bank[0], bank[1]]
        vA = [[bank[2], bank[3]], [bank[4], bank[5]]]
        u_ps = [bank[0], bank[3]]
        r_ps = [bank[1], bank[4]]
        xg_ps = [bank[2], bank[5]]
        g_ps = xg_ps
        keep_ps = r_ps
        hg_ps = bank[6]
        tp_ps = bank[7]
        attT_lo_ps = [bank[3], bank[4]]
        attT_hi_ps = bank[5]
        fin_ps = [bank[7], bank[0]]

        ident_zero = sem("ident_zero")
        ident_ready = sem("ident_ready")
        weights_in = sem("weights_in")
        watt_in = sem("watt_in")
        targ0_in = sem("targ0_in")
        setup_T = sem("setup_T")
        setup_out = sem("setup_out")
        w_hi_ready = sem("w_hi_ready")
        hist_in = [[sem(f"hist_in{c}{g}") for g in range(HALVES)] for c in range(2)]
        targ_in = [[sem(f"targ_in{c}{g}") for g in range(HALVES)] for c in range(2)]
        a_tp = sem("a_tp")
        a_histT = sem("a_histT")
        a_v = sem("a_v")
        a_dots = sem("a_dots")
        a_sum = sem("a_sum")
        sm_max = sem("sm_max")
        sm_exp = sem("sm_exp")
        sm_inv = sem("sm_inv")
        sm_att = sem("sm_att")
        att_tp = sem("att_tp")
        attT_lo_out = sem("attT_lo_out")
        attT_hi_out = sem("attT_hi_out")
        att_out = sem("att_out")
        att_in = [[sem(f"att_in{c}{q}") for q in range(2)] for c in range(2)]
        tp_done = sem("tp_done")
        xhi_done = sem("xhi_done")
        xlo_done = sem("xlo_done")
        r_mm = sem("r_mm")
        g_mm = sem("g_mm")
        u_mm = sem("u_mm")
        r_done = sem("r_done")
        u_done = sem("u_done")
        ua_done = sem("ua_done")
        rg_done = sem("rg_done")
        pre_done = sem("pre_done")
        g_done = sem("g_done")
        ug_done = sem("ug_done")
        h_done = sem("h_done")
        hhi_done = sem("hhi_done")
        hlo_done = sem("hlo_done")
        fin_mm = sem("fin_mm")
        fin_out = [sem(f"fin_out{g}") for g in range(HALVES)]
        stored = sem("stored")

        block = ctx.enter_context(nc.Block())

        XU, XR, XG, HU, HR, HG = range(6)

        @block.sync
        def _(sp):
            def load(buf, src, done, t0, c, g):
                blocks = slice(g * HB, (g + 1) * HB)
                sp.dma_start(buf[c][:, blocks, :, :], src[:, blocks, bass.ds(t0 + c * TC, TC), :])\
                    .then_inc(done[c][g], DMA)

            sp.dma_start(w_att[:, 0:H], W_w).then_inc(watt_in, DMA)
            for c in range(2):
                for g in range(HALVES):
                    load(hist_buf, hist_v, hist_in, 0, c, g)
                    load(targ_buf, targets_v, targ_in, 0, c, g)
                    if c == g == 0:
                        sp.dma_start(w_att[:, H:H + 1], W_b.rearrange("(p a) -> p a", a=1)).then_inc(watt_in, DMA)

            for j, w in enumerate((xu_w, xr_w, xg_w, hu_w, hr_w, hg_w)):
                sp.dma_start(w_nat[:, j, :], w).then_inc(weights_in, DMA)
            for j, b in enumerate((xu_b, hu_b, xr_b, hr_b, xg_b, hg_b)):
                sp.dma_start(bias[:, j:j + 1], b.rearrange("(p a) -> p a", a=1)).then_inc(weights_in, DMA)
            sp.dma_start(ln2_nat[:, :], ln2_w).then_inc(weights_in, DMA)
            sp.dma_start(ln2_row[:, :], ln2_b.rearrange("(a n) -> a n", a=1)).then_inc(weights_in, DMA)
            sp.dma_start(targ0[:, :, :], targets_v[:, :, 0, :]).then_inc(targ0_in, DMA)

            with nc.Fori(1, ITERS, engines=(ENGINE.SP,), hint_back_edge=True) as i:
                for c in range(2):
                    for g in range(HALVES):
                        left = UNITS - (c * CU + (g + 1) * TC)
                        sp.wait_ge(a_tp, i * UNITS - left)
                        load(hist_buf, hist_v, hist_in, i * BODY, c, g)
                        sp.wait_ge(a_dots, i * UNITS + (2 - left))
                        load(targ_buf, targets_v, targ_in, i * BODY, c, g)

            for c in range(2):
                for g in range(HALVES):
                    sp.wait_ge(a_tp, T * HALVES - UNITS + c * CU + (g + 1) * TC)
                    load(hist_buf, hist_v, hist_in, 0, c, g)

            def load_att(t0, c):
                for q in range(2):
                    sp.dma_start(att_bc[c][:, 2 * q:2 * q + 2, :],
                                 att_dram[bass.ds(t0 + c * TC + 2 * q, 2), :].partition_broadcast(P))\
                        .then_inc(att_in[c][q], DMA)

            sp.wait_ge(attT_lo_out, 2)
            sp.dma_start(att_dram[0:TLO, :], attT_lo[:, :]).then_inc(att_out, DMA)
            sp.wait_ge(attT_hi_out, 2)
            sp.dma_start(att_dram[TLO:T, :], attT_hi[:, :]).then_inc(att_out, DMA)
            sp.wait_ge(att_out, 2 * DMA)
            for c in range(2):
                load_att(0, c)
            with nc.Fori(1, ITERS, engines=(ENGINE.SP,), hint_back_edge=True) as i:
                for c in range(2):
                    left = UNITS - (c + 1) * CU
                    sp.wait_ge(tp_done, i * UNITS - left)
                    for g in range(HALVES):
                        load(hist_buf, hist_v, hist_in, i * BODY, c, g)
                    sp.wait_ge(ua_done, i * UNITS - left)
                    load_att(i * BODY, c)

            for g in range(HALVES):
                sp.wait_ge(fin_out[g], 1)
                sp.dma_start(out_v[:, g * HB:(g + 1) * HB, :], out_sb[:, g * HB:(g + 1) * HB, :])\
                    .then_inc(stored, DMA)
            sp.wait_ge(stored, 2 * DMA)

        @block.gpsimd
        def _(pool):
            nc.gpsimd.memset(ident[:, :], 0.0).then_inc(ident_zero, 1)
            pool.wait_ge(ident_zero, 1)
            nc.gpsimd.affine_select(out=ident[:, :], in_=ident[:, :], compare_op=ALU.not_equal, fill=1.0,
                                    base=0, pattern=[[-1, P]], channel_multiplier=1).then_inc(ident_ready, 1)

            def unit(i, j, last):
                n, g, c, tt = i * UNITS + j, j % 2, j // CU, j % CU // 2
                if g == 0 and tt % 2 == 0:
                    pool.wait_ge(att_in[c][tt // 2], (i + 1) * DMA)
                pool.wait_ge(u_done, n + 1)
                nc.gpsimd.tensor_tensor(ua_sb[g][:, :], u_sb[g][:, :], att_bc[c][:, tt, g * N:(g + 1) * N],
                                        ALU.mult).then_inc(ua_done, 1)
                if not (last and j == UNITS - 1):
                    pool.wait_ge(hhi_done, n + 2)
                    nc.gpsimd.tensor_tensor(h_lo[1 - g][:, :], h_all[1 - g][:, :],
                                            h_hi[1 - g][:, :].bitcast(F32), ALU.subtract).then_inc(hlo_done, 1)

            with nc.Fori(0, ITERS - 1, engines=(ENGINE.Pool,), hint_back_edge=True) as i:
                for j in range(UNITS):
                    unit(i, j, False)
            for j in range(UNITS):
                unit(ITERS - 1, j, True)

        @block.tensor
        def _(pe):
            def transpose_history(g, c, tt, dst, done):
                for k in range(HB):
                    last = nc.tensor.transpose(dst[:, k * P:(k + 1) * P], hist_buf[c][:, g * HB + k, tt, :],
                                               ident[:, :])
                last.then_inc(done, 1)

            def unit_a(i, j, last):
                n = i * UNITS + j
                if not (last and j + 1 == UNITS):
                    ahead = (j + 1) % UNITS
                    c, g, tt = ahead // CU, ahead % CU // TC, ahead % TC
                    if tt == 0:
                        pe.wait_ge(hist_in[c][g], (i + (1 + (j + 1) // UNITS)) * DMA)
                    transpose_history(g, c, tt, tpA[ahead % 2], a_tp)
                pe.wait_ge(a_histT, n + 1)
                pe.wait_ge(a_dots, n + 1)
                for k in range(HB):
                    last = nc.tensor.matmul(vA[j % 2][k // 2][:, k % 2 * VC:k % 2 * VC + H + 1],
                                            histT[j % 2][:, k * P:(k + 1) * P], w_att[:, :],
                                            start=True, stop=True)
                last.then_inc(a_v, 1)

            pe.wait_ge(ident_ready, 1)
            pe.wait_ge(hist_in[0][0], DMA)
            transpose_history(0, 0, 0, tpA[0], a_tp)
            pe.wait_ge(watt_in, 2 * DMA)
            with nc.Fori(0, ITERS - 1, engines=(ENGINE.PE,), hint_back_edge=True) as i:
                for j in range(UNITS):
                    unit_a(i, j, False)
            for j in range(UNITS):
                unit_a(ITERS - 1, j, True)

            pe.wait_ge(weights_in, 14 * DMA)
            for q in range(2):
                if q:
                    pe.wait_ge(setup_out, q)
                for j in range(3):
                    last = nc.tensor.transpose(setup_ps[:, j * H:(j + 1) * H], w_nat[:, 3 * q + j, :], ident[:, :])
                last.then_inc(setup_T, 1)

            for q in range(HALVES):
                pe.wait_ge(sm_att, q + 1)
                for k in range(HB):
                    last = nc.tensor.transpose(attT_lo_ps[q][:, k * P:(k + 1) * P],
                                               scores[:, q * HB + k, 0:TLO], ident[:, :])
                last.then_inc(att_tp, 1)
                if q:
                    pe.wait_ge(attT_hi_out, q)
                for k in range(HB):
                    last = nc.tensor.transpose(attT_hi_ps[0:THI, k * P:(k + 1) * P],
                                               scores[:, q * HB + k, TLO:T], ident[:, :])
                last.then_inc(att_tp, 1)

            def from_history(g, banks):
                for dst, w in banks:
                    nc.tensor.matmul(dst[:, :], w_lo[:, w, :], x_hi[g][:, :], start=True, stop=False)
                    nc.tensor.matmul(dst[:, :], w_hi[:, w, :], x_hi[g][:, :], start=False, stop=False)
                    nc.tensor.matmul(dst[:, :], w_hi[:, w, :], x_lo[g][:, :], start=False, stop=w == XG)

            def unit(i, j, last):
                n, g = i * UNITS + j, j % 2
                pe.wait_ge(hhi_done, n + 1)
                pe.wait_ge(rg_done, n + 1)
                gates = ((u_ps[g], HU), (r_ps[g], HR), (hg_ps, HG))
                for dst, w in gates:
                    nc.tensor.matmul(dst[:, :], w_hi[:, w, :], h_hi[g][:, :], start=w == HG, stop=False)
                    nc.tensor.matmul(dst[:, :], w_lo[:, w, :], h_hi[g][:, :], start=False, stop=False)
                pe.wait_ge(hlo_done, n + 1)
                for (dst, w), ready in zip(gates, (u_mm, r_mm, g_mm)):
                    nc.tensor.matmul(dst[:, :], w_hi[:, w, :], h_lo[g][:, :], start=False, stop=True)\
                        .then_inc(ready, 1)
                if last and j + 1 == UNITS:
                    return
                pe.wait_ge(xlo_done, n + 2)
                if not (last and j + 2 >= UNITS):
                    ahead = (j + 2) % UNITS
                    c, tt = ahead // CU, ahead % CU // 2
                    if tt == 0:
                        pe.wait_ge(hist_in[c][g], (i + (ITERS + 1 + (j + 2) // UNITS)) * DMA)
                    transpose_history(g, c, tt, tp_ps, tp_done)
                from_history(1 - g, [(u_ps[1 - g], XU)])
                pe.wait_ge(ug_done, n + 1)
                from_history(1 - g, [(xg_ps[1 - g], XG)])
                pe.wait_ge(h_done, n + 2)
                from_history(1 - g, [(r_ps[1 - g], XR)])

            pe.wait_ge(setup_out, 2)
            pe.wait_ge(hist_in[0][0], (ITERS + 1) * DMA)
            transpose_history(0, 0, 0, tp_ps, tp_done)

            for j in range(2):
                last = nc.tensor.transpose(out_setup_ps[:, j * H:(j + 1) * H], ln2_nat[:, j * H:(j + 1) * H],
                                           ident[:, :])
            last.then_inc(setup_T, 1)
            pe.wait_ge(targ0_in, DMA)
            for q in range(HALVES):
                pe.wait_ge(setup_out, 3 + q)
                for k in range(HB):
                    last = nc.tensor.transpose(out_setup_ps[:, k * P:(k + 1) * P], targ0[:, q * HB + k, :],
                                               ident[:, :])
                last.then_inc(setup_T, 1)

            pe.wait_ge(xlo_done, 1)
            pe.wait_ge(hist_in[0][1], (ITERS + 1) * DMA)
            transpose_history(1, 0, 0, tp_ps, tp_done)
            from_history(0, [(u_ps[0], XU), (xg_ps[0], XG), (r_ps[0], XR)])
            pe.wait_ge(setup_out, 5)
            pe.wait_ge(attT_lo_out, 2)
            pe.wait_ge(attT_hi_out, 2)
            with nc.Fori(0, ITERS - 1, engines=(ENGINE.PE,), hint_back_edge=True) as i:
                for j in range(UNITS):
                    unit(i, j, False)
            for j in range(UNITS):
                unit(ITERS - 1, j, True)

            for g in range(HALVES):
                if g == 0:
                    pe.wait_ge(xlo_done, T * HALVES)
                else:
                    pe.wait_ge(u_done, T * HALVES - 1)
                for k in range(HB):
                    nc.tensor.matmul(fin_ps[g][:, k * P:(k + 1) * P],
                                     targ0_T[:, (g * HB + k) * P:(g * HB + k + 1) * P], ln2_T[:, H:2 * H],
                                     start=k == 0, stop=False)
                for k in range(HB):
                    nc.tensor.matmul(fin_ps[g][:, k * P:(k + 1) * P], ones_row[:, :], ln2_row[:, :],
                                     start=False, stop=False)
            for g in range(HALVES):
                pe.wait_ge(h_done, T * HALVES + 1 + g)
                for k in range(HB):
                    last = nc.tensor.matmul(fin_ps[g][:, k * P:(k + 1) * P], h_all[g][:, k * P:(k + 1) * P],
                                            ln2_T[:, 0:H], start=False, stop=k == HB - 1)
                last.then_inc(fin_mm, 1)

        @block.scalar
        def _(act):
            nc.scalar.preload_act_table(ACT.Exp)
            with nc.Fori(0, ITERS, engines=(ENGINE.Activation,), hint_back_edge=True) as i:
                for j in range(UNITS):
                    act.wait_ge(a_tp, i * UNITS + (j + 1))
                    nc.scalar.activation(histT[j % 2][:, :], tpA[j % 2][:, :], ACT.Copy).then_inc(a_histT, 1)

            for q in range(2):
                act.wait_ge(setup_T, q + 1)
                nc.scalar.activation(w_hi[:, 3 * q:3 * q + 3, :], setup_ps[:, 0:3 * H], ACT.Copy)\
                    .then_inc(w_hi_ready, 1)

            act.wait_ge(sm_max, 2)
            for q in range(HALVES):
                for k in range(q * HB, (q + 1) * HB):
                    last = nc.scalar.activation(scores[:, k, :], scores[:, k, :], ACT.Exp,
                                                bias=neg_max[:, k:k + 1], accum_out=exp_sum[:, k:k + 1])
                last.then_inc(sm_exp, 1)

            nc.scalar.preload_act_table(ACT.Sigmoid)

            for q in range(HALVES):
                act.wait_ge(att_tp, 2 * q + 1)
                nc.scalar.activation(attT_lo[:, q * N:(q + 1) * N], attT_lo_ps[q][:, :], ACT.Copy)\
                    .then_inc(attT_lo_out, 1)

            def split_history(n, g):
                act.wait_ge(tp_done, n + 1)
                nc.scalar.activation(x_hi[g][:, :], tp_ps[:, :], ACT.Copy).then_inc(xhi_done, 1)

            def unit(i, j, last):
                n, g = i * UNITS + j, j % 2
                act.wait_ge(u_mm, n + 1)
                nc.scalar.activation(u_sb[g][:, :], u_ps[g][:, :], ACT.Sigmoid, bias=bias[:, 6:7]).then_inc(u_done, 1)
                act.wait_ge(r_mm, n + 1)
                nc.scalar.activation(r_sb[g][:, :], r_ps[g][:, :], ACT.Sigmoid, bias=bias[:, 7:8]).then_inc(r_done, 1)
                if not (last and j == UNITS - 1):
                    act.wait_ge(h_done, n + 2)
                    nc.scalar.activation(h_hi[1 - g][:, :], h_all[1 - g][:, :], ACT.Copy).then_inc(hhi_done, 1)
                if not (last and j + 2 >= UNITS):
                    split_history(n + 2, g)
                act.wait_ge(pre_done, n + 1)
                nc.scalar.activation(g_ps[g][:, :], pre_sb[g][:, :], ACT.Tanh, bias=bias[:, 4:5]).then_inc(g_done, 1)

            split_history(0, 0)
            act.wait_ge(setup_T, 3)
            nc.scalar.activation(ln2_T[:, :], out_setup_ps[:, 0:2 * H], ACT.Copy).then_inc(setup_out, 1)
            for q in range(HALVES):
                act.wait_ge(setup_T, 4 + q)
                nc.scalar.activation(targ0_T[:, q * N:(q + 1) * N], out_setup_ps[:, :], ACT.Copy)\
                    .then_inc(setup_out, 1)
            split_history(1, 1)
            with nc.Fori(0, ITERS - 1, engines=(ENGINE.Activation,), hint_back_edge=True) as i:
                for j in range(UNITS):
                    unit(i, j, False)
            for j in range(UNITS):
                unit(ITERS - 1, j, True)

            act.wait_ge(fin_mm, 1)
            nc.scalar.activation(out_sb[:, 0:HB, :], fin_ps[0][:, :], ACT.Copy).then_inc(fin_out[0], 1)

        @block.vector
        def _(dve):
            nc.vector.memset(ones_row[:, :], 1.0).then_inc(a_sum, 1)
            for g in range(HALVES):
                nc.vector.memset(h_all[g][:, :], 0.0).then_inc(h_done, 1)
            nc.vector.memset(h_hi[0][:, :].bitcast(F32), 0.0).then_inc(hhi_done, 1)
            nc.vector.memset(h_lo[0][:, :].bitcast(F32), 0.0).then_inc(hlo_done, 1)

            for g in range(HALVES):
                nc.vector.memset(prod_junk[:, g, :, :], 0.0).then_inc(a_dots, 1)
            with nc.Fori(0, ITERS, engines=(ENGINE.DVE,), hint_back_edge=True) as i:
                dve.wait_ge(a_sum, i + 1)
                for j in range(UNITS):
                    c, g, tt = j // CU, j % CU // TC, j % TC
                    if tt == 0:
                        dve.wait_ge(targ_in[c][g], (i + 1) * DMA)
                    dve.wait_ge(a_v, i * UNITS + (j + 1))
                    for k in range(HB):
                        v = vA[j % 2][k // 2][:, k % 2 * VC:k % 2 * VC + H + 1]
                        step = c * TC + tt
                        last = nc.vector.tensor_tensor_reduce(
                            out=prod_junk[:, j % 2, k, :], in0=v[:, 0:H],
                            in1=targ_buf[c][:, g * HB + k, tt, :], scale=1.0, scalar=v[:, H:H + 1],
                            op0=ALU.mult, op1=ALU.add, accum_out=s_dots[:, g * HB + k, step:step + 1])
                    last.then_inc(a_dots, 1)
                dve.wait_ge(a_dots, i * UNITS + (UNITS + 2))
                nc.vector.tensor_copy(scores[:, :, bass.ds(i * BODY, BODY)], s_dots[:, :, :]).then_inc(a_sum, 1)

            dve.wait_ge(a_sum, ITERS + 1)
            nc.vector.reduce_max(neg_max[:, :], scores[:, :, :], AX.X).then_inc(sm_max, 1)
            dve.wait_ge(sm_max, 1)
            nc.vector.tensor_scalar(neg_max[:, :], neg_max[:, :], -1.0, None, ALU.mult).then_inc(sm_max, 1)
            for q in range(2):
                dve.wait_ge(w_hi_ready, q + 1)
                nc.vector.tensor_tensor(w_lo[:, 3 * q:3 * q + 3, :],
                                        setup_ps[:, 0:3 * H].rearrange("p (j h) -> p j h", j=3),
                                        w_hi[:, 3 * q:3 * q + 3, :].bitcast(F32), ALU.subtract)\
                    .then_inc(setup_out, 1)
            dve.wait_ge(weights_in, 14 * DMA)
            nc.vector.tensor_tensor(bias[:, 6:7], bias[:, 0:1], bias[:, 1:2], ALU.add).then_inc(ug_done, 1)
            nc.vector.tensor_tensor(bias[:, 7:8], bias[:, 2:3], bias[:, 3:4], ALU.add).then_inc(rg_done, 1)
            for q in range(HALVES):
                dve.wait_ge(sm_exp, q + 1)
                nc.vector.reciprocal(exp_inv[:, q * HB:(q + 1) * HB], exp_sum[:, q * HB:(q + 1) * HB])\
                    .then_inc(sm_inv, 1)
                dve.wait_ge(sm_inv, q + 1)
                for k in range(q * HB, (q + 1) * HB):
                    last = nc.vector.tensor_scalar(scores[:, k, :], scores[:, k, :], exp_inv[:, k:k + 1], None,
                                                   ALU.mult)
                last.then_inc(sm_att, 1)
            for q in range(HALVES):
                dve.wait_ge(att_tp, 2 * q + 2)
                nc.vector.tensor_copy(attT_hi[:, q * N:(q + 1) * N], attT_hi_ps[0:THI, :]).then_inc(attT_hi_out, 1)

            def split_history(n, g):
                dve.wait_ge(xhi_done, n + 1)
                nc.vector.tensor_tensor(x_lo[g][:, :], tp_ps[:, :], x_hi[g][:, :].bitcast(F32), ALU.subtract)\
                    .then_inc(xlo_done, 1)

            def unit(i, j, last):
                n, g = i * UNITS + j, j % 2
                dve.wait_ge(g_mm, n + 1)
                dve.wait_ge(r_done, n + 1)
                nc.vector.scalar_tensor_tensor(out=rg_sb[g][:, :], in0=hg_ps[:, :], scalar=bias[:, 5:6],
                                               in1=r_sb[g][:, :], op0=ALU.add, op1=ALU.mult).then_inc(rg_done, 1)
                dve.wait_ge(rg_done, n + 2)
                nc.vector.tensor_tensor(pre_sb[g][:, :], rg_sb[g][:, :], xg_ps[g][:, :], ALU.add)\
                    .then_inc(pre_done, 1)
                if not (last and j + 2 >= UNITS):
                    split_history(n + 2, g)
                dve.wait_ge(ua_done, n + 1)
                nc.vector.scalar_tensor_tensor(out=keep_ps[g][:, :], in0=ua_sb[g][:, :], scalar=-1.0,
                                               in1=h_all[g][:, :], op0=ALU.add, op1=ALU.mult)
                dve.wait_ge(g_done, n + 1)
                nc.vector.tensor_tensor(ug_sb[g][:, :], ua_sb[g][:, :], g_ps[g][:, :], ALU.mult).then_inc(ug_done, 1)
                dve.wait_ge(ug_done, n + 2)
                nc.vector.tensor_tensor(h_all[g][:, :], ug_sb[g][:, :], keep_ps[g][:, :], ALU.subtract)\
                    .then_inc(h_done, 1)

            split_history(0, 0)
            split_history(1, 1)
            with nc.Fori(0, ITERS - 1, engines=(ENGINE.DVE,), hint_back_edge=True) as i:
                for j in range(UNITS):
                    unit(i, j, False)
            for j in range(UNITS):
                unit(ITERS - 1, j, True)

            dve.wait_ge(fin_mm, 2)
            nc.vector.tensor_copy(out_sb[:, HB:BLK, :], fin_ps[1][:, :].rearrange("p (k o) -> p k o", k=HB))\
                .then_inc(fin_out[1], 1)


_INS = ["r_targets", "r_history_states"] + [
    f"L0_rec_{w}_{k}" for w in ("W", "xu", "hu", "xr", "hr", "xg", "hg", "ln2") for k in "wb"]
_OUT = ((1024, 128), "float32")


def kernel(**inputs):
    import numpy as np
    import concourse.bacc as bacc
    from concourse.bass_utils import run_bass_kernel_spmd

    nc = bacc.Bacc("TRN2", target_bir_lowering=False, num_devices=1)
    arrays, args = {}, []
    for name in _INS:
        a = np.ascontiguousarray(inputs[name])
        arrays[f"in_{name}"] = a
        args.append(nc.dram_tensor(f"in_{name}", a.shape, mybir.dt.from_np(a.dtype), kind="ExternalInput").ap())
    args.append(nc.dram_tensor("out_dram", _OUT[0], mybir.dt.from_np(np.dtype(_OUT[1])), kind="ExternalOutput").ap())
    bass_attention_gru(nc, *args)
    r = run_bass_kernel_spmd(nc, [arrays], core_ids=[0])
    return r.results[0]["out_dram"]
```
